# Optimizing a Trainium2 kernel written in Bass

```python
import numpy as np
import jax
import jax.numpy as jnp

def _softmax(x, axis=-1):
    return jax.nn.softmax(x, axis=axis)

def _gelu(x):
    return jax.nn.gelu(x, approximate=True)

def _silu(x):
    return jax.nn.silu(x)

def _sigmoid(x):
    return jax.nn.sigmoid(x)

def _layernorm(x, axis=-1, eps=1e-05):
    m = jnp.mean(x, axis=axis, keepdims=True)
    v = jnp.var(x, axis=axis, keepdims=True)
    return (x - m) / jnp.sqrt(v + eps)

def _scatter_add(tgt, idx, src, axis=0):
    return tgt.at[idx].add(src)

def _segment_sum(src, seg, n):
    return jax.ops.segment_sum(src, seg, n)
kernel_name = 'mk_adj_preln_d1_adj_r2_957e18'

def setup_inputs(seed: int=0):
    np.random.seed(seed)
    _w = jnp.asarray

    def _rec_inputs():
        import jax
        import jax.numpy as jnp
        _gk = jax.random.key(seed)
        x = -0.0002928 + 1 * jax.random.normal(jax.random.fold_in(_gk, 1), (16, 512, 256), jnp.float32)
        _a = jax.random.bernoulli(jax.random.fold_in(_gk, 2), 0.015625, (512, 512))
        _af = _a.astype(jnp.float32)
        adj = _af
        return (x, adj)
    x, adj = _rec_inputs()

    def _L0_gnn_setup():
        import jax, jax.numpy as jnp
        import numpy as np
        B, N, D, H = (4, 1024, 256, 8)
        HD = D // H
        key = jax.random.key(seed)
        ks = jax.random.split(key, 10)
        x = jax.random.normal(ks[0], (B, N, D), dtype=jnp.float32)
        adj = (jax.random.uniform(ks[1], (N, N)) < 0.1).astype(jnp.float32)
        s = 1.0 / np.sqrt(D)
        Wq = jax.random.normal(ks[2], (D, D), dtype=jnp.float32) * s
        Wk = jax.random.normal(ks[3], (D, D), dtype=jnp.float32) * s
        Wv = jax.random.normal(ks[4], (D, D), dtype=jnp.float32) * s
        Wo = jax.random.normal(ks[5], (D, D), dtype=jnp.float32) * s
        bq = jnp.zeros((D,), jnp.float32)
        bk = jnp.zeros((D,), jnp.float32)
        bv = jnp.zeros((D,), jnp.float32)
        bo = jnp.zeros((D,), jnp.float32)
        return {'x': x, 'adj': adj, 'Wq': Wq, 'bq': bq, 'Wk': Wk, 'bk': bk, 'Wv': Wv, 'bv': bv, 'Wo': Wo, 'bo': bo}
    _L0_gnn_all = _L0_gnn_setup()
    _L0_gnn_in = {k: v for k, v in _L0_gnn_all.items() if k in ('Wq', 'bq', 'Wk', 'bk', 'Wv', 'bv', 'Wo', 'bo')}
    del _L0_gnn_all
    return {'x': x, 'adj': adj, 'L0_gnn_Wq': _L0_gnn_in['Wq'], 'L0_gnn_bq': _L0_gnn_in['bq'], 'L0_gnn_Wk': _L0_gnn_in['Wk'], 'L0_gnn_bk': _L0_gnn_in['bk'], 'L0_gnn_Wv': _L0_gnn_in['Wv'], 'L0_gnn_bv': _L0_gnn_in['bv'], 'L0_gnn_Wo': _L0_gnn_in['Wo'], 'L0_gnn_bo': _L0_gnn_in['bo']}

def reference(x, adj, L0_gnn_Wq, L0_gnn_bq, L0_gnn_Wk, L0_gnn_bk, L0_gnn_Wv, L0_gnn_bv, L0_gnn_Wo, L0_gnn_bo):
    import jax
    import jax.numpy as jnp

    def _L0_gnn_ref(x, adj, Wq, bq, Wk, bk, Wv, bv, Wo, bo):
        import jax, jax.numpy as jnp
        import numpy as np
        B, N, D, H = (4, 1024, 256, 8)
        HD = D // H
        b, n, d = x.shape
        q = (x @ Wq + bq).reshape(b, n, H, HD)
        k = (x @ Wk + bk).reshape(b, n, H, HD)
        v = (x @ Wv + bv).reshape(b, n, H, HD)
        scores = jnp.einsum('bqhd,bkhd->bhqk', q, k) / jnp.sqrt(jnp.float32(HD))
        scores = scores + (1.0 - adj)[None, None, :, :] * -1000000000.0
        attn = jax.nn.softmax(scores, axis=-1)
        out = jnp.einsum('bhqk,bkhd->bqhd', attn, v).reshape(b, n, d)
        return out @ Wo + bo
    h = jnp.maximum(_layernorm(x, axis=-1), 0.0)
    x = x + _L0_gnn_ref(h, adj, L0_gnn_Wq, L0_gnn_bq, L0_gnn_Wk, L0_gnn_bk, L0_gnn_Wv, L0_gnn_bv, L0_gnn_Wo, L0_gnn_bo)
    return x

_drawn_inputs = setup_inputs


def setup_inputs(seed=0):
    import zlib

    import numpy as np

    out = dict(_drawn_inputs(seed))
    spreads = {'L0_gnn_bq': (0.0, 0.724),
     'L0_gnn_bk': (0.0, 0.8),
     'L0_gnn_bv': (0.0, 0.1),
     'L0_gnn_bo': (0.0, 0.1)}
    factors = {}
    for name, (base, spread) in spreads.items():
        noise = np.random.default_rng([zlib.crc32(name.encode()), seed]).standard_normal(out[name].shape)
        drawn = base * np.exp(spread * noise) if base else spread * noise
        out[name] = jnp.asarray(drawn.astype(out[name].dtype))
    for name, factor in factors.items():
        out[name] = (out[name] * factor).astype(out[name].dtype)
    return out
```

```python
import math
from contextlib import ExitStack

import concourse.bass as bass
from concourse import mybir

HEADS = 8
MASKED = 1e9
EPS = 1e-5


def gnn_attention(nc, x, adj, Wq, bq, Wk, bk, Wv, bv, Wo, bo, out):
    fp32 = mybir.dt.float32
    fp32r = mybir.dt.float32r
    ALU = mybir.AluOpType
    ACT = mybir.ActivationFunctionType

    B, N, D = x.shape
    P = 128
    HD = D // HEADS
    TT = N // P
    DT = D // P
    G = P // HD
    UNITS = HEADS * TT
    GU = G * TT
    SCALE = 1.0 / math.sqrt(HD)
    LAG = 3
    SR = 4
    assert N == 512 and D == 256 and UNITS == 32 and GU == 16

    JOB_AT = {0: "cq1", 1: "ck1", 11: "ps1", 12: "cv0", 14: "cv1", 16: "nh0", 17: "nh1",
              21: "nq0", 22: "nk0", 24: "po0", 26: "po1", 28: "cs0"}
    JOBS = [j[1:] for j in JOB_AT.values()]
    BANK = {j: i % 2 for i, j in enumerate(JOBS)}
    OFFSET = {j[1:]: {"p": -1, "c": 0, "n": 1}[j[0]] for j in JOB_AT.values()}
    PV_AT = {4: (1, 0), 6: (1, 1), 8: (1, 2), 10: (1, 3), 20: (0, 0), 23: (0, 1), 25: (0, 2), 27: (0, 3)}

    x_tiles = x.rearrange("b (t p) d -> b p t d", p=P)
    out_tiles = out.rearrange("b (t p) d -> b p t d", p=P)

    ctx = ExitStack()
    with ctx:
        def sb(name, shape, dt=fp32):
            return ctx.enter_context(nc.sbuf_tensor(name, shape, dt))

        def sem(name):
            return ctx.enter_context(nc.semaphore(name))

        ident = sb("ident", [P, P])
        mask = sb("mask", [P, TT, N])
        w_raw = {w: sb(f"w{w}_raw", [P, DT, D]) for w in "qkvo"}
        w_hi = {w: sb(f"w{w}_hi", [P, DT, D], fp32r) for w in "qkv"}
        w_lo = {w: sb(f"w{w}_lo", [P, DT, D], fp32r) for w in "qkv"}
        b_col = {w: sb(f"b{w}_col", [P, DT]) for w in "qk"}
        bv_row = sb("bv_row", [P, D])
        bo_row = sb("bo_row", [P, D])
        x_in = sb("x_in", [P, TT, D])
        stats = sb("stats", [P, TT, 6])
        mean_var = sb("mean_var", [P, TT, 2])
        var_eps = sb("var_eps", [P, TT])
        minus_half = sb("minus_half", [P, TT])
        rs_guess = sb("rs_guess", [P, TT])
        rs_square = sb("rs_square", [P, TT])
        rs_error = sb("rs_error", [P, TT])
        rs_factor = sb("rs_factor", [P, TT])
        rstd = sb("rstd", [P, TT])
        normed = sb("normed", [P, TT, D])
        hT_hi = sb("hT_hi", [P, DT, N], fp32r)
        hT_lo = sb("hT_lo", [P, DT, N], fp32r)
        part_hi = {w: sb(f"{w}_hi", [P, N], fp32r) for w in "qk"}
        part_lo = {w: sb(f"{w}_lo", [P, N], fp32r) for w in "qk"}
        stack = {(w, g): sb(f"{w}_stack{g}", [P, G, N], fp32r) for w in "qk" for g in range(DT)}
        v_sb = sb("v_sb", [P, TT, D])
        scores = sb("scores", [P, SR, N])
        neg_max = sb("neg_max", [P, UNITS])
        probs = sb("probs", [P, SR, N])
        row_sum = sb("row_sum", [P, UNITS])
        row_inv = sb("row_inv", [P, UNITS])
        probsT = [sb(f"probsT{g}", [P, G, TT, N]) for g in range(DT)]
        inv_spread = [sb(f"inv_spread{g}", [P, N]) for g in range(DT)]
        attnT = [sb(f"attnT{g}", [P, N]) for g in range(DT)]
        x_res = sb("x_res", [P, TT, D])
        x_bias = sb("x_bias", [P, TT, D])
        y = sb("y", [P, TT, D])

        def bank(name):
            return ctx.enter_context(nc.psum_tensor(name, [P, N], fp32))

        ps_scores = [bank(f"ps_scores{i}") for i in range(2)]
        ps_turn = [bank(f"ps_turn{i}") for i in range(2)]
        ps_attn = [bank(f"ps_attn{g}") for g in range(DT)]
        ps_job = [bank(f"ps_job{i}") for i in range(2)]

        loaded = {n: sem(f"loaded_{n}") for n in ("adj", "w", "bias")}
        ident_ready = sem("ident_ready")
        consts_ready = sem("consts_ready")
        scaled_ready = sem("scaled_ready")
        split_hi_ready = sem("split_hi_ready")
        weights_ready = sem("weights_ready")
        x_loaded = sem("x_loaded")
        res_loaded = sem("res_loaded")
        stats_ready = sem("stats_ready")
        mean_var_ready = sem("mean_var_ready")
        rs_step = sem("rs_step")
        normed_ready = sem("normed_ready")
        res_ready = sem("res_ready")
        job_done = {j: sem(f"job_done_{j}") for j in JOBS}
        job_hi = {j: sem(f"job_hi_{j}") for j in JOBS if j[0] in "qkh"}
        job_taken = {j: sem(f"job_taken_{j}") for j in JOBS}
        stacked = {j: sem(f"stacked_{j}") for j in JOBS if j[0] in "qk"}
        scores_done = sem("scores_done")
        masked_ready = sem("masked_ready")
        probs_ready = sem("probs_ready")
        turned = sem("turned")
        turn_taken = [sem("turn_taken_dve"), sem("turn_taken_act")]
        inv_ready = [sem(f"inv_ready{g}") for g in range(DT)]
        attn_done = [sem(f"attn_done{g}") for g in range(DT)]
        attn_ready = [sem(f"attn_ready{g}") for g in range(DT)]
        stored = sem("stored")

        def job_before(b, j):
            at = (b - OFFSET[j]) * len(JOBS) + JOBS.index(j) - 2
            while at > -len(JOBS):
                before = JOBS[at % len(JOBS)]
                its = at // len(JOBS) + OFFSET[before]
                if 0 <= its < B:
                    return before, its
                at -= 2
            return j, -1

        def wait(eng, s, value):
            if not isinstance(value, int) or value > 0:
                eng.wait_ge(s, value)

        def whole(eng, body):
            body(-1, False, False, True)
            body(0, False, True, True)
            for b in range(1, B - 1):
                body(b, True, True, True)
            body(B - 1, True, True, False)
            body(B, True, False, False)

        block = ctx.enter_context(nc.Block())

        @block.sync
        def _(sp):
            sp.dma_start(x_in[:, :, :], x_tiles[0]).then_inc(x_loaded, 16)
            for w, src in zip("qkvo", (Wq, Wk, Wv, Wo)):
                sp.dma_start(w_raw[w][:, :, :], src.rearrange("(t p) n -> p t n", p=P)).then_inc(loaded["w"], 16)
            sp.dma_start(b_col["q"][:, :], bq.rearrange("(t p) -> p t", p=P),
                         allow_slow_non_contiguous=True).then_inc(loaded["bias"], 16)
            sp.dma_start(b_col["k"][:, :], bk.rearrange("(t p) -> p t", p=P),
                         allow_slow_non_contiguous=True).then_inc(loaded["bias"], 16)
            sp.dma_start(bv_row[:, :], bv.partition_broadcast(P)).then_inc(loaded["bias"], 16)
            sp.dma_start(bo_row[:, :], bo.partition_broadcast(P)).then_inc(loaded["bias"], 16)
            sp.dma_start(mask[:, :, :], adj.rearrange("(t p) k -> p t k", p=P)).then_inc(loaded["adj"], 16)

            def stack_up(job, b):
                w, g = job[0], int(job[1])
                wait(sp, scores_done, b * UNITS - (GU if g == 0 else 0))
                wait(sp, job_taken[job], b + 1)
                for r in range(G):
                    lo = r >= 2 if w == "q" else r % 2 == 1
                    src = (part_lo if lo else part_hi)[w]
                    for j in range(G):
                        sp.dma_start(stack[w, g][r * HD:(r + 1) * HD, j, :].bitcast(fp32),
                                     src[j * HD:(j + 1) * HD, :].bitcast(fp32)).then_inc(stacked[job], 16)

            def body(b, prev, cur, nxt):
                if nxt and cur:
                    wait(sp, normed_ready, (b + 1) * TT)
                    sp.dma_start(x_in[:, :, :], x_tiles[b + 1]).then_inc(x_loaded, 16)
                if prev:
                    wait(sp, res_ready, b - 1)
                    sp.dma_start(x_res[:, :, :], x_tiles[b - 1]).then_inc(res_loaded, 16)
                if cur:
                    stack_up("q1", b)
                    stack_up("k1", b)
                if nxt:
                    stack_up("q0", b + 1)
                    stack_up("k0", b + 1)
                if prev:
                    wait(sp, job_taken["o0"], b)
                    wait(sp, job_taken["o1"], b)
                    sp.dma_start(out_tiles[b - 1], y[:, :, :]).then_inc(stored, 16)

            whole(sp, body)
            sp.wait_ge(stored, 16 * B)

        @block.gpsimd
        def _(pool):
            pool.memset(ident[:, :], 0.0).then_inc(ident_ready, 1)
            pool.wait_ge(ident_ready, 1)
            pool.affine_select(out=ident[:, :], in_=ident[:, :], compare_op=ALU.not_equal, fill=1.0,
                               base=0, pattern=[[-1, P]], channel_multiplier=1).then_inc(ident_ready, 1)
            pool.memset(minus_half[:, :], -0.5).then_inc(consts_ready, 1)
            pool.wait_ge(consts_ready, 1)
            STEPS = 6

            def body(b, prev, cur, nxt):
                if nxt:
                    done = (b + 1) * STEPS
                    wait(pool, mean_var_ready, (b + 2) * TT)
                    pool.tensor_scalar(var_eps[:, :], mean_var[:, :, 1], EPS, None, ALU.add).then_inc(rs_step, 1)
                    wait(pool, rs_step, done + 1)
                    pool.tensor_tensor(rs_guess[:, :], var_eps[:, :], minus_half[:, :], ALU.pow).then_inc(rs_step, 1)
                    wait(pool, rs_step, done + 2)
                    pool.tensor_tensor(rs_square[:, :], rs_guess[:, :], rs_guess[:, :], ALU.mult).then_inc(rs_step, 1)
                    wait(pool, rs_step, done + 3)
                    pool.tensor_tensor(rs_error[:, :], rs_square[:, :], var_eps[:, :], ALU.mult).then_inc(rs_step, 1)
                    wait(pool, rs_step, done + 4)
                    pool.tensor_scalar(rs_factor[:, :], rs_error[:, :], -0.5, 1.5, ALU.mult, ALU.add).then_inc(rs_step, 1)
                    wait(pool, rs_step, done + 5)
                    pool.tensor_tensor(rstd[:, :], rs_guess[:, :], rs_factor[:, :], ALU.mult).then_inc(rs_step, 1)
                    wait(pool, rs_step, done + 6)
                    wait(pool, job_done["h1"], b + 1)
                    for t in range(TT):
                        pool.tensor_scalar(normed[:, t, :], x_in[:, t, :], mean_var[:, t, 0:1], rstd[:, t:t + 1],
                                           ALU.subtract, ALU.mult).then_inc(normed_ready, 1)
                if prev:
                    wait(pool, res_loaded, 16 * b)
                    wait(pool, job_taken["o1"], b - 1)
                    pool.wait_ge(loaded["bias"], 64)
                    pool.tensor_tensor(x_bias[:, :, :], x_res[:, :, :],
                                       bo_row[:, :].unsqueeze(1).to_broadcast([P, TT, D]), ALU.add).then_inc(res_ready, 1)

            whole(pool, body)

        @block.tensor
        def _(pe):
            pe.wait_ge(ident_ready, 2)
            pe.wait_ge(weights_ready, 3)

            def score(b, u):
                g, j, t = u // GU, u % GU // TT, u % TT
                if u % GU == 0:
                    wait(pe, stacked[f"q{g}"], (b + 1) * 16 * G * G)
                    wait(pe, stacked[f"k{g}"], (b + 1) * 16 * G * G)
                wait(pe, masked_ready, b * UNITS + u - 1)
                pe.matmul(ps_scores[u % 2][:, :], stack["q", g][:, j, t * P:(t + 1) * P], stack["k", g][:, j, :],
                          start=True, stop=True).then_inc(scores_done, 1)

            def turn(b, u):
                wait(pe, probs_ready, b * UNITS + u + 1)
                wait(pe, turn_taken[u % 2], b * UNITS // 2 + u // 2)
                for k in range(TT):
                    mm = pe.transpose(ps_turn[u % 2][:, k * P:(k + 1) * P], probs[:, u % SR, k * P:(k + 1) * P],
                                      ident[:, :])
                mm.then_inc(turned, 1)

            def attend(b, g, k):
                if k == 0:
                    for taken in turn_taken:
                        wait(pe, taken, b * UNITS // 2 + (g + 1) * GU // 2)
                    wait(pe, job_taken["v0"], b + 1)
                    wait(pe, job_taken["v1"], b + 1)
                    wait(pe, attn_ready[g], b)
                for j in range(G):
                    h = g * G + j
                    mm = pe.matmul(ps_attn[g][j * HD:(j + 1) * HD, :], v_sb[:, k, h * HD:(h + 1) * HD],
                                   probsT[g][:, j, k, :], start=(k == 0), stop=(k == TT - 1))
                if k == TT - 1:
                    mm.then_inc(attn_done[g], 1)

            def split_products(dst, pairs):
                todo = [(a, r) for (ah, al), (rh, rl) in pairs for a, r in ((ah, rh), (ah, rl), (al, rh))]
                for n, (a, r) in enumerate(todo):
                    mm = pe.matmul(dst, a, r, start=(n == 0), stop=(n == len(todo) - 1))
                return mm

            def job(b, j):
                kind, n = j[0], int(j[1])
                dst = ps_job[BANK[j]]
                before, its = job_before(b, j)
                wait(pe, job_taken[before], its + 1)
                if kind == "h":
                    wait(pe, normed_ready, (b + 1) * TT)
                    for t in range(TT):
                        mm = pe.transpose(dst[:, t * P:(t + 1) * P], normed[:, t, n * P:(n + 1) * P], ident[:, :])
                elif kind in "qk":
                    wait(pe, job_taken["h0"], b + 1)
                    wait(pe, job_taken["h1"], b + 1)
                    cols = slice(n * P, (n + 1) * P)
                    mm = split_products(dst[:, :], [((w_hi[kind][:, d, cols], w_lo[kind][:, d, cols]),
                                                     (hT_hi[:, d, :], hT_lo[:, d, :])) for d in range(DT)])
                elif kind == "v":
                    for i in range(2):
                        rows = slice((2 * n + i) * P, (2 * n + i + 1) * P)
                        mm = split_products(dst[:, i * D:(i + 1) * D],
                                            [((hT_hi[:, d, rows], hT_lo[:, d, rows]),
                                              (w_hi["v"][:, d, :], w_lo["v"][:, d, :])) for d in range(DT)])
                elif kind == "s":
                    wait(pe, inv_ready[n], b + 1)
                    for t in range(TT):
                        for i in range(G):
                            u = n * GU + i * TT + t
                            mm = pe.matmul(dst[i * HD:(i + 1) * HD, t * P:(t + 1) * P],
                                           row_inv[:, u:u + 1].to_broadcast([P, HD]), ident[:, :],
                                           start=True, stop=True)
                elif kind == "o":
                    for g in range(DT):
                        wait(pe, attn_ready[g], b + 1)
                    for i in range(2):
                        rows = slice((2 * n + i) * P, (2 * n + i + 1) * P)
                        for g in range(DT):
                            mm = pe.matmul(dst[:, i * D:(i + 1) * D], attnT[g][:, rows], w_raw["o"][:, g, :],
                                           start=(g == 0), stop=(g == DT - 1))
                mm.then_inc(job_done[j], 1)

            def body(b, prev, cur, nxt):
                there = {"p": prev, "c": cur, "n": nxt}
                for slot in range(UNITS):
                    if cur:
                        score(b, slot)
                    if slot < LAG and prev:
                        turn(b - 1, slot - LAG + UNITS)
                    if slot >= LAG and cur:
                        turn(b, slot - LAG)
                    if slot in PV_AT:
                        g, k = PV_AT[slot]
                        if prev and g == 1:
                            attend(b - 1, g, k)
                        if cur and g == 0:
                            attend(b, g, k)
                    if slot in JOB_AT and there[JOB_AT[slot][0]]:
                        j = JOB_AT[slot][1:]
                        job(b + OFFSET[j], j)

            whole(pe, body)

        @block.vector
        def _(dve):
            dve.wait_ge(loaded["w"], 64)
            dve.wait_ge(loaded["bias"], 64)
            dve.tensor_scalar(w_raw["q"][:, :, :], w_raw["q"][:, :, :], -SCALE, None, ALU.mult).then_inc(scaled_ready, 1)
            dve.tensor_scalar(b_col["q"][:, :], b_col["q"][:, :], -SCALE, None, ALU.mult).then_inc(scaled_ready, 1)
            dve.wait_ge(scaled_ready, 2)
            for n, w in enumerate("qkv"):
                dve.tensor_copy(w_hi[w][:, :, :], w_raw[w][:, :, :]).then_inc(split_hi_ready, 1)
                dve.wait_ge(split_hi_ready, n + 1)
                dve.tensor_tensor(w_lo[w][:, :, :], w_raw[w][:, :, :], w_hi[w][:, :, :].bitcast(fp32),
                                  ALU.subtract).then_inc(weights_ready, 1)
            dve.wait_ge(loaded["adj"], 16)
            dve.tensor_scalar(mask[:, :, :], mask[:, :, :], 1.0, -MASKED, ALU.subtract, ALU.mult).then_inc(scaled_ready, 1)
            dve.wait_ge(scaled_ready, 3)

            def masked(b, u):
                wait(dve, scores_done, b * UNITS + u + 1)
                wait(dve, probs_ready, b * UNITS + u - SR + 1)
                dve.tensor_tensor_reduce(scores[:, u % SR, :], ps_scores[u % 2][:, :], mask[:, u % TT, :], 1.0, 3e38,
                                         ALU.add, ALU.min, neg_max[:, u:u + 1]).then_inc(masked_ready, 1)

            def take_turned(b, u):
                g, j, t = u // GU, u % GU // TT, u % TT
                wait(dve, turned, b * UNITS + u + 1)
                if u % GU == 0:
                    wait(dve, attn_done[g], b)
                dve.tensor_copy(probsT[g][:, j, :, t * P:(t + 1) * P],
                                ps_turn[u % 2][:, :].rearrange("p (k q) -> p k q", q=P)).then_inc(turn_taken[0], 1)

            def low_part(b, j):
                w, g = j[0], int(j[1])
                wait(dve, job_hi[j], b + 1)
                dve.scalar_tensor_tensor(out=part_lo[w][:, :], in0=ps_job[BANK[j]][:, :], scalar=b_col[w][:, g:g + 1],
                                         in1=part_hi[w][:, :].bitcast(fp32), op0=ALU.add,
                                         op1=ALU.subtract).then_inc(job_taken[j], 1)

            def low_h(b, j):
                d = int(j[1])
                wait(dve, job_hi[j], b + 1)
                dve.scalar_tensor_tensor(out=hT_lo[:, d, :], in0=ps_job[BANK[j]][:, :], scalar=0.0,
                                         in1=hT_hi[:, d, :].bitcast(fp32), op0=ALU.max,
                                         op1=ALU.subtract).then_inc(job_taken[j], 1)

            def take_v(b, j):
                n = int(j[1])
                wait(dve, job_done[j], b + 1)
                wait(dve, attn_done[1], b)
                dve.tensor_tensor(v_sb[:, 2 * n:2 * n + 2, :], ps_job[BANK[j]][:, :].rearrange("p (t n) -> p t n", n=D),
                                  bv_row[:, :].unsqueeze(1).to_broadcast([P, 2, D]), ALU.add).then_inc(job_taken[j], 1)

            def invert(b, g):
                wait(dve, probs_ready, b * UNITS + (g + 1) * GU)
                wait(dve, job_done[f"s{g}"], b)
                dve.reciprocal(row_inv[:, g * GU:(g + 1) * GU], row_sum[:, g * GU:(g + 1) * GU]).then_inc(inv_ready[g], 1)

            def normalize(b, g):
                wait(dve, attn_done[g], b + 1)
                wait(dve, job_taken[f"s{g}"], b + 1)
                wait(dve, job_done["o1"], b)
                dve.tensor_tensor(attnT[g][:, :], ps_attn[g][:, :], inv_spread[g][:, :], ALU.mult).then_inc(attn_ready[g], 1)

            def take_out(b, j):
                n = int(j[1])
                wait(dve, job_done[j], b + 1)
                wait(dve, res_ready, b + 1)
                wait(dve, stored, b * 16)
                dve.tensor_tensor(y[:, 2 * n:2 * n + 2, :], ps_job[BANK[j]][:, :].rearrange("p (t n) -> p t n", n=D),
                                  x_bias[:, 2 * n:2 * n + 2, :], ALU.add).then_inc(job_taken[j], 1)

            def moments(b, t):
                if t == 0:
                    wait(dve, x_loaded, (b + 1) * 16)
                    wait(dve, normed_ready, b * TT)
                dve.bn_stats(stats[:, t, :], x_in[:, t, :]).then_inc(stats_ready, 1)

            def aggregate(b, t):
                wait(dve, stats_ready, b * TT + t + 1)
                dve.bn_aggr(mean_var[:, t, :], stats[:, t, :]).then_inc(mean_var_ready, 1)

            def body(b, prev, cur, nxt):
                for slot in range(UNITS):
                    if cur:
                        masked(b, slot)
                    u = (slot - LAG) % UNITS
                    if u % 2 == 0:
                        if slot < LAG and prev:
                            take_turned(b - 1, u)
                        if slot >= LAG and cur:
                            take_turned(b, u)
                    if slot == 2 and cur:
                        low_part(b, "q1")
                    if slot == 3 and cur:
                        low_part(b, "k1")
                    if slot == 4 and prev:
                        invert(b - 1, 1)
                    if 5 <= slot < 5 + TT and nxt:
                        moments(b + 1, slot - 5)
                    if 6 <= slot < 6 + TT and nxt:
                        aggregate(b + 1, slot - 6)
                    if slot == 13 and prev:
                        normalize(b - 1, 1)
                    if slot == 13 and cur:
                        take_v(b, "v0")
                    if slot == 15 and cur:
                        take_v(b, "v1")
                    if slot == 18 and nxt:
                        low_h(b + 1, "h0")
                    if slot == 19 and nxt:
                        low_h(b + 1, "h1")
                    if slot == 20 and cur:
                        invert(b, 0)
                    if slot == 23 and nxt:
                        low_part(b + 1, "q0")
                    if slot == 24 and nxt:
                        low_part(b + 1, "k0")
                    if slot == 25 and prev:
                        take_out(b - 1, "o0")
                    if slot == 27 and prev:
                        take_out(b - 1, "o1")
                    if slot == 30 and cur:
                        normalize(b, 0)

            whole(dve, body)

        @block.scalar
        def _(act):
            act.wait_ge(scaled_ready, 2)

            def exponential(b, u):
                wait(act, masked_ready, b * UNITS + u + 1)
                wait(act, turned, b * UNITS + u - SR + 1)
                if u % GU == 0:
                    wait(act, inv_ready[u // GU], b)
                act.activation(probs[:, u % SR, :], scores[:, u % SR, :], ACT.Exp, bias=neg_max[:, u:u + 1],
                               scale=-1.0, accum_out=row_sum[:, u:u + 1]).then_inc(probs_ready, 1)

            def take_turned(b, u):
                g, j, t = u // GU, u % GU // TT, u % TT
                wait(act, turned, b * UNITS + u + 1)
                if u % GU == 1:
                    wait(act, attn_done[g], b)
                act.activation(probsT[g][:, j, :, t * P:(t + 1) * P],
                               ps_turn[u % 2][:, :].rearrange("p (k q) -> p k q", q=P),
                               ACT.Copy).then_inc(turn_taken[1], 1)

            def high_part(b, j):
                w, g = j[0], int(j[1])
                wait(act, job_done[j], b + 1)
                wait(act, stacked[f"{w}{1 - g}"], (b + g) * 16 * G * G)
                act.activation(part_hi[w][:, :], ps_job[BANK[j]][:, :], ACT.Identity,
                               bias=b_col[w][:, g:g + 1]).then_inc(job_hi[j], 1)

            def high_h(b, j):
                d = int(j[1])
                wait(act, job_done[j], b + 1)
                wait(act, job_done["v1"], b)
                act.activation(hT_hi[:, d, :], ps_job[BANK[j]][:, :], ACT.Relu).then_inc(job_hi[j], 1)

            def take_spread(b, g):
                j = f"s{g}"
                wait(act, job_done[j], b + 1)
                wait(act, attn_ready[g], b)
                act.activation(inv_spread[g][:, :], ps_job[BANK[j]][:, :], ACT.Copy).then_inc(job_taken[j], 1)

            def body(b, prev, cur, nxt):
                for slot in range(UNITS):
                    if cur:
                        exponential(b, slot)
                    u = (slot - LAG) % UNITS
                    if u % 2 == 1:
                        if slot < LAG and prev:
                            take_turned(b - 1, u)
                        if slot >= LAG and cur:
                            take_turned(b, u)
                    if slot == 1 and cur:
                        high_part(b, "q1")
                    if slot == 2 and cur:
                        high_part(b, "k1")
                    if slot == 12 and prev:
                        take_spread(b - 1, 1)
                    if slot == 17 and nxt:
                        high_h(b + 1, "h0")
                    if slot == 18 and nxt:
                        high_h(b + 1, "h1")
                    if slot == 22 and nxt:
                        high_part(b + 1, "q0")
                    if slot == 23 and nxt:
                        high_part(b + 1, "k0")
                    if slot == 29 and cur:
                        take_spread(b, 0)

            whole(act, body)


_INS = ['x', 'adj', 'L0_gnn_Wq', 'L0_gnn_bq', 'L0_gnn_Wk', 'L0_gnn_bk', 'L0_gnn_Wv', 'L0_gnn_bv', 'L0_gnn_Wo',
        'L0_gnn_bo']


def kernel(**inputs):
    import numpy as _np
    import concourse.bacc as _bacc
    from concourse import mybir as _mybir
    from concourse.bass_utils import run_bass_kernel_spmd as _run

    nc = _bacc.Bacc("TRN2", target_bir_lowering=False, num_devices=1)
    arrays, args = {}, []
    for name in _INS:
        a = _np.ascontiguousarray(inputs[name])
        arrays[f"in_{name}_dram"] = a
        args.append(nc.dram_tensor(f"in_{name}_dram", a.shape, _mybir.dt.from_np(a.dtype), kind="ExternalInput").ap())
    args.append(nc.dram_tensor("out_0_dram", arrays["in_x_dram"].shape, _mybir.dt.float32, kind="ExternalOutput").ap())
    gnn_attention(nc, *args)
    r = _run(nc, [arrays], core_ids=[0])
    return r.results[0]["out_0_dram"]
```

```python
import math
from contextlib import ExitStack

import concourse.bass as bass
from concourse import mybir

HEADS = 8
MASKED = 1e9
EPS = 1e-5


def gnn_attention(nc, x, adj, Wq, bq, Wk, bk, Wv, bv, Wo, bo, out):
    fp32 = mybir.dt.float32
    fp32r = mybir.dt.float32r
    ALU = mybir.AluOpType
    ACT = mybir.ActivationFunctionType

    B, N, D = x.shape
    P = 128
    HD = D // HEADS
    TT = N // P
    DT = D // P
    G = P // HD
    UNITS = HEADS * TT
    GU = G * TT
    SCALE = 1.0 / math.sqrt(HD)
    LAG = 3
    SB = 3
    SR = 4
    assert N == 512 and D == 256 and UNITS == 32 and GU == 16

    JOB_AT = {0: "cq1a", 1: "cq1b", 2: "ck1a", 3: "ck1b", 5: "cv0a", 6: "cv0b", 8: "cv1a", 9: "cv1b",
              10: "nh0", 12: "nh1", 14: "ps1", 15: "nq0a", 16: "nq0b", 17: "nk0a", 18: "nk0b",
              19: "po0a", 20: "po0b", 22: "po1a", 23: "po1b", 28: "cs0"}
    JOBS = list(dict.fromkeys(j[1:3] for j in JOB_AT.values()))
    BANK = {j: i % 2 for i, j in enumerate(JOBS)}
    OFFSET = {j[1:3]: {"p": -1, "c": 0, "n": 1}[j[0]] for j in JOB_AT.values()}
    PV_AT = {4: (1, 0), 7: (1, 1), 11: (1, 2), 13: (1, 3), 21: (0, 0), 24: (0, 1), 26: (0, 2), 29: (0, 3)}
    TAKER = [1 if u % 2 == 1 or u % 16 == 8 else 0 for u in range(UNITS)]


    x_tiles = x.rearrange("b (t p) d -> b p t d", p=P)
    out_tiles = out.rearrange("b (t p) d -> b p t d", p=P)

    ctx = ExitStack()
    with ctx:
        def sb(name, shape, dt=fp32):
            return ctx.enter_context(nc.sbuf_tensor(name, shape, dt))

        def sem(name):
            return ctx.enter_context(nc.semaphore(name))

        ident = sb("ident", [P, P])
        mask = sb("mask", [P, TT, N])
        w_raw = {w: sb(f"w{w}_raw", [P, DT, D]) for w in "qkvo"}
        w_hi = {w: sb(f"w{w}_hi", [P, DT, D], fp32r) for w in "qkv"}
        w_lo = {w: sb(f"w{w}_lo", [P, DT, D], fp32r) for w in "qkv"}
        b_col = {w: sb(f"b{w}_col", [P, DT]) for w in "qk"}
        bv_row = sb("bv_row", [P, D])
        bo_row = sb("bo_row", [P, D])
        x_in = sb("x_in", [P, TT, D])
        stats = sb("stats", [P, TT, 6])
        mean_var = sb("mean_var", [P, TT, 2])
        var_eps = sb("var_eps", [P, TT])
        minus_half = sb("minus_half", [P, TT])
        rs_guess = sb("rs_guess", [P, TT])
        rs_square = sb("rs_square", [P, TT])
        rs_error = sb("rs_error", [P, TT])
        rs_factor = sb("rs_factor", [P, TT])
        rstd = sb("rstd", [P, TT])
        normed = sb("normed", [P, TT, D])
        hT_hi = sb("hT_hi", [P, DT, N], fp32r)
        hT_lo = sb("hT_lo", [P, DT, N], fp32r)
        parts = sb("parts", [P, 4, N], fp32r)
        part_hi = {"q": parts[:, 0, :], "k": parts[:, 3, :]}
        part_lo = {"q": parts[:, 1, :], "k": parts[:, 2, :]}
        stacks = [sb(f"stacks{g}", [P, 2, G, N], fp32r) for g in range(DT)]
        v_sb = [sb(f"v_sb{i}", [P, TT, D]) for i in range(2)]
        scores = sb("scores", [P, SR, N])
        neg_max = sb("neg_max", [P, UNITS])
        probs = sb("probs", [P, SR, N])
        row_sum = sb("row_sum", [P, UNITS])
        row_inv = sb("row_inv", [P, UNITS])
        probsT = [sb(f"probsT{g}", [P, G, TT, N]) for g in range(DT)]
        inv_spread = [sb(f"inv_spread{g}", [P, N]) for g in range(DT)]
        attnT = [sb(f"attnT{g}", [P, N]) for g in range(DT)]
        x_res = sb("x_res", [P, TT, D])
        x_bias = sb("x_bias", [P, TT, D])
        y = sb("y", [P, TT, D])

        def bank(name):
            return ctx.enter_context(nc.psum_tensor(name, [P, N], fp32))

        ps_scores = [bank(f"ps_scores{i}") for i in range(SB)]
        ps_turn = [bank(f"ps_turn{i}") for i in range(2)]
        ps_attn = bank("ps_attn")
        ps_job = [bank(f"ps_job{i}") for i in range(2)]

        loaded = {n: sem(f"loaded_{n}") for n in ("adj", "w", "bias")}
        ident_ready = sem("ident_ready")
        consts_ready = sem("consts_ready")
        scaled_ready = sem("scaled_ready")
        split_hi_ready = sem("split_hi_ready")
        weights_ready = sem("weights_ready")
        x_loaded = sem("x_loaded")
        res_loaded = sem("res_loaded")
        stats_ready = sem("stats_ready")
        mean_var_ready = sem("mean_var_ready")
        rs_step = sem("rs_step")
        normed_ready = sem("normed_ready")
        res_ready = sem("res_ready")
        job_done = {j: sem(f"job_done_{j}") for j in JOBS}
        job_hi = {j: sem(f"job_hi_{j}") for j in JOBS if j[0] in "qkh"}
        job_taken = {j: sem(f"job_taken_{j}") for j in JOBS}
        stacked = [sem(f"stacked{g}") for g in range(DT)]
        scores_done = sem("scores_done")
        masked_ready = sem("masked_ready")
        probs_ready = sem("probs_ready")
        turned = sem("turned")
        turn_taken = [sem("turn_taken_dve"), sem("turn_taken_act")]
        inv_ready = [sem(f"inv_ready{g}") for g in range(DT)]
        attn_done = [sem(f"attn_done{g}") for g in range(DT)]
        attn_ready = [sem(f"attn_ready{g}") for g in range(DT)]
        stored = sem("stored")

        def taken(b, u, by):
            return b * TAKER.count(by) + TAKER[:u].count(by)

        def job_before(b, j):
            at = (b - OFFSET[j]) * len(JOBS) + JOBS.index(j) - 2
            while at > -len(JOBS):
                before = JOBS[at % len(JOBS)]
                its = at // len(JOBS) + OFFSET[before]
                if has(its):
                    return before, its
                at -= 2
            return j, -1

        def wait(eng, s, value):
            if not isinstance(value, int) or value > 0:
                eng.wait_ge(s, value)

        def has(b):
            return 0 <= b < B

        block = ctx.enter_context(nc.Block())

        @block.sync
        def _(sp):
            sp.dma_start(x_in[:, :, :], x_tiles[0]).then_inc(x_loaded, 16)
            for w, src in zip("qkvo", (Wq, Wk, Wv, Wo)):
                sp.dma_start(w_raw[w][:, :, :], src.rearrange("(t p) n -> p t n", p=P)).then_inc(loaded["w"], 16)
            sp.dma_start(b_col["q"][:, :], bq.rearrange("(t p) -> p t", p=P),
                         allow_slow_non_contiguous=True).then_inc(loaded["bias"], 16)
            sp.dma_start(b_col["k"][:, :], bk.rearrange("(t p) -> p t", p=P),
                         allow_slow_non_contiguous=True).then_inc(loaded["bias"], 16)
            sp.dma_start(bv_row[:, :], bv.partition_broadcast(P)).then_inc(loaded["bias"], 16)
            sp.dma_start(bo_row[:, :], bo.partition_broadcast(P)).then_inc(loaded["bias"], 16)
            sp.dma_start(mask[:, :, :], adj.rearrange("(t p) k -> p t k", p=P)).then_inc(loaded["adj"], 16)

            def stack_up(b, g):
                wait(sp, scores_done, (b - 1) * UNITS + (g + 1) * GU)
                wait(sp, job_taken[f"q{g}"], b + 1)
                wait(sp, job_taken[f"k{g}"], b + 1)
                for j in range(G):
                    for r, (a, z, step) in enumerate(((0, 4, 3), (0, 3, 2), (1, 4, 2), (1, 3, 1))):
                        sp.dma_start(stacks[g][r * HD:(r + 1) * HD, :, j, :].bitcast(fp32),
                                     parts[j * HD:(j + 1) * HD, a:z:step, :].bitcast(fp32)).then_inc(stacked[g], 16)

            def load_x(b):
                wait(sp, normed_ready, b * TT)
                sp.dma_start(x_in[:, :, :], x_tiles[b]).then_inc(x_loaded, 16)

            def load_residual(b):
                wait(sp, res_ready, b)
                sp.dma_start(x_res[:, :, :], x_tiles[b]).then_inc(res_loaded, 16)

            def store(b):
                wait(sp, job_taken["o0"], b + 1)
                wait(sp, job_taken["o1"], b + 1)
                sp.dma_start(out_tiles[b], y[:, :, :]).then_inc(stored, 16)

            for b in range(-1, B + 1):
                if has(b - 1):
                    load_residual(b - 1)
                if has(b):
                    stack_up(b, 1)
                if has(b + 2):
                    load_x(b + 2)
                if has(b + 1):
                    stack_up(b + 1, 0)
                if has(b - 1):
                    store(b - 1)
            sp.wait_ge(stored, 16 * B)

        @block.gpsimd
        def _(pool):
            pool.memset(ident[:, :], 0.0).then_inc(ident_ready, 1)
            pool.wait_ge(ident_ready, 1)
            pool.affine_select(out=ident[:, :], in_=ident[:, :], compare_op=ALU.not_equal, fill=1.0,
                               base=0, pattern=[[-1, P]], channel_multiplier=1).then_inc(ident_ready, 1)
            pool.memset(minus_half[:, :], -0.5).then_inc(consts_ready, 1)
            pool.wait_ge(consts_ready, 1)
            STEPS = 6

            def norm(b):
                done = b * STEPS
                wait(pool, mean_var_ready, (b + 1) * TT)
                pool.tensor_scalar(var_eps[:, :], mean_var[:, :, 1], EPS, None, ALU.add).then_inc(rs_step, 1)
                wait(pool, rs_step, done + 1)
                pool.tensor_tensor(rs_guess[:, :], var_eps[:, :], minus_half[:, :], ALU.pow).then_inc(rs_step, 1)
                wait(pool, rs_step, done + 2)
                pool.tensor_tensor(rs_square[:, :], rs_guess[:, :], rs_guess[:, :], ALU.mult).then_inc(rs_step, 1)
                wait(pool, rs_step, done + 3)
                pool.tensor_tensor(rs_error[:, :], rs_square[:, :], var_eps[:, :], ALU.mult).then_inc(rs_step, 1)
                wait(pool, rs_step, done + 4)
                pool.tensor_scalar(rs_factor[:, :], rs_error[:, :], -0.5, 1.5, ALU.mult, ALU.add).then_inc(rs_step, 1)
                wait(pool, rs_step, done + 5)
                pool.tensor_tensor(rstd[:, :], rs_guess[:, :], rs_factor[:, :], ALU.mult).then_inc(rs_step, 1)
                wait(pool, rs_step, done + 6)
                wait(pool, job_done["h1"], b)
                for t in range(TT):
                    pool.tensor_scalar(normed[:, t, :], x_in[:, t, :], mean_var[:, t, 0:1], rstd[:, t:t + 1],
                                       ALU.subtract, ALU.mult).then_inc(normed_ready, 1)

            def residual(b):
                wait(pool, res_loaded, 16 * (b + 1))
                wait(pool, job_taken["o1"], b)
                pool.wait_ge(loaded["bias"], 64)
                pool.tensor_tensor(x_bias[:, :, :], x_res[:, :, :],
                                   bo_row[:, :].unsqueeze(1).to_broadcast([P, TT, D]), ALU.add).then_inc(res_ready, 1)

            for b in range(-2, B + 1):
                if has(b - 1):
                    residual(b - 1)
                if has(b + 2):
                    norm(b + 2)

        @block.tensor
        def _(pe):
            pe.wait_ge(ident_ready, 2)
            pe.wait_ge(weights_ready, 3)

            def score(b, u):
                g, j, t = u // GU, u % GU // TT, u % TT
                if u % GU == 0:
                    wait(pe, stacked[g], (b + 1) * 16 * G * G)
                wait(pe, masked_ready, b * UNITS + u + 1 - SB)
                pe.matmul(ps_scores[(b * UNITS + u) % SB][:, :], stacks[g][:, 0, j, t * P:(t + 1) * P], stacks[g][:, 1, j, :],
                          start=True, stop=True).then_inc(scores_done, 1)

            def turn(b, u):
                wait(pe, probs_ready, b * UNITS + u + 1)
                last = (u - 2) % UNITS
                by = TAKER[last]
                wait(pe, turn_taken[by], taken(b if u >= 2 else b - 1, last + 1, by))
                for k in range(TT):
                    mm = pe.transpose(ps_turn[u % 2][:, k * P:(k + 1) * P], probs[:, u % SR, k * P:(k + 1) * P],
                                      ident[:, :])
                mm.then_inc(turned, 1)

            def attend(b, g, k):
                if k == 0:
                    for by in range(2):
                        wait(pe, turn_taken[by], taken(b, (g + 1) * GU, by))
                    wait(pe, job_taken["v0"], b + 1)
                    wait(pe, job_taken["v1"], b + 1)
                    wait(pe, attn_ready[1 - g], b + g)
                for j in range(G):
                    h = g * G + j
                    mm = pe.matmul(ps_attn[j * HD:(j + 1) * HD, :], v_sb[b % 2][:, k, h * HD:(h + 1) * HD],
                                   probsT[g][:, j, k, :], start=(k == 0), stop=(k == TT - 1))
                if k == TT - 1:
                    mm.then_inc(attn_done[g], 1)

            def split_products(dst, pairs, first=True, last=True):
                todo = [(a, r) for (ah, al), (rh, rl) in pairs for a, r in ((ah, rh), (ah, rl), (al, rh))]
                for n, (a, r) in enumerate(todo):
                    mm = pe.matmul(dst, a, r, start=(first and n == 0), stop=(last and n == len(todo) - 1))
                return mm

            def job(b, j, halves):
                kind, n = j[0], int(j[1])
                dst = ps_job[BANK[j]]
                if 0 in halves:
                    before, its = job_before(b, j)
                    wait(pe, job_taken[before], its + 1)
                if kind == "h":
                    wait(pe, normed_ready, (b + 1) * TT)
                    for t in range(TT):
                        mm = pe.transpose(dst[:, t * P:(t + 1) * P], normed[:, t, n * P:(n + 1) * P], ident[:, :])
                elif kind in "qk":
                    wait(pe, job_taken["h0"], b + 1)
                    wait(pe, job_taken["h1"], b + 1)
                    cols = slice(n * P, (n + 1) * P)
                    for d in halves:
                        mm = split_products(dst[:, :], [((w_hi[kind][:, d, cols], w_lo[kind][:, d, cols]),
                                                         (hT_hi[:, d, :], hT_lo[:, d, :]))], d == 0, d == DT - 1)
                elif kind == "v":
                    for i in halves:
                        rows = slice((2 * n + i) * P, (2 * n + i + 1) * P)
                        mm = split_products(dst[:, i * D:(i + 1) * D],
                                            [((hT_hi[:, d, rows], hT_lo[:, d, rows]),
                                              (w_hi["v"][:, d, :], w_lo["v"][:, d, :])) for d in range(DT)])
                elif kind == "s":
                    wait(pe, inv_ready[n], b + 1)
                    for t in range(TT):
                        for i in range(G):
                            u = n * GU + i * TT + t
                            mm = pe.matmul(dst[i * HD:(i + 1) * HD, t * P:(t + 1) * P],
                                           row_inv[:, u:u + 1].to_broadcast([P, HD]), ident[:, :],
                                           start=True, stop=True)
                elif kind == "o":
                    for g in range(DT):
                        wait(pe, attn_ready[g], b + 1)
                    for i in halves:
                        rows = slice((2 * n + i) * P, (2 * n + i + 1) * P)
                        for g in range(DT):
                            mm = pe.matmul(dst[:, i * D:(i + 1) * D], attnT[g][:, rows], w_raw["o"][:, g, :],
                                           start=(g == 0), stop=(g == DT - 1))
                if 1 in halves:
                    mm.then_inc(job_done[j], 1)

            for b in range(-1, B + 1):
                for slot in range(UNITS):
                    if has(b):
                        score(b, slot)
                    its = b if slot >= LAG else b - 1
                    if has(its):
                        turn(its, (slot - LAG) % UNITS)
                    if slot in PV_AT:
                        g, k = PV_AT[slot]
                        if has(b - g):
                            attend(b - g, g, k)
                    if slot in JOB_AT:
                        j, half = JOB_AT[slot][1:3], JOB_AT[slot][3:]
                        if has(b + OFFSET[j]):
                            job(b + OFFSET[j], j, {"": (0, 1), "a": (0,), "b": (1,)}[half])

        @block.vector
        def _(dve):
            dve.wait_ge(loaded["w"], 64)
            dve.wait_ge(loaded["bias"], 64)
            dve.tensor_scalar(w_raw["q"][:, :, :], w_raw["q"][:, :, :], -SCALE, None, ALU.mult).then_inc(scaled_ready, 1)
            dve.tensor_scalar(b_col["q"][:, :], b_col["q"][:, :], -SCALE, None, ALU.mult).then_inc(scaled_ready, 1)
            dve.wait_ge(scaled_ready, 2)
            for n, w in enumerate("qkv"):
                dve.tensor_copy(w_hi[w][:, :, :], w_raw[w][:, :, :]).then_inc(split_hi_ready, 1)
                dve.wait_ge(split_hi_ready, n + 1)
                dve.tensor_tensor(w_lo[w][:, :, :], w_raw[w][:, :, :], w_hi[w][:, :, :].bitcast(fp32),
                                  ALU.subtract).then_inc(weights_ready, 1)
            dve.wait_ge(loaded["adj"], 16)
            dve.tensor_scalar(mask[:, :, :], mask[:, :, :], 1.0, -MASKED, ALU.subtract, ALU.mult).then_inc(scaled_ready, 1)
            dve.wait_ge(scaled_ready, 3)

            def masked(b, u):
                wait(dve, scores_done, b * UNITS + u + 1)
                wait(dve, probs_ready, b * UNITS + u - SR + 1)
                dve.tensor_tensor_reduce(scores[:, u % SR, :], ps_scores[(b * UNITS + u) % SB][:, :], mask[:, u % TT, :], 1.0, 3e38,
                                         ALU.add, ALU.min, neg_max[:, u:u + 1]).then_inc(masked_ready, 1)

            def take_turned(b, u):
                g, j, t = u // GU, u % GU // TT, u % TT
                wait(dve, turned, b * UNITS + u + 1)
                if u % GU == 0:
                    wait(dve, attn_done[g], b)
                dve.tensor_copy(probsT[g][:, j, :, t * P:(t + 1) * P],
                                ps_turn[u % 2][:, :].rearrange("p (k q) -> p k q", q=P)).then_inc(turn_taken[0], 1)

            def low_part(b, j):
                w, g = j[0], int(j[1])
                wait(dve, job_hi[j], b + 1)
                dve.scalar_tensor_tensor(out=part_lo[w], in0=ps_job[BANK[j]][:, :], scalar=b_col[w][:, g:g + 1],
                                         in1=part_hi[w].bitcast(fp32), op0=ALU.add,
                                         op1=ALU.subtract).then_inc(job_taken[j], 1)

            def low_h(b, j):
                d = int(j[1])
                wait(dve, job_hi[j], b + 1)
                dve.scalar_tensor_tensor(out=hT_lo[:, d, :], in0=ps_job[BANK[j]][:, :], scalar=0.0,
                                         in1=hT_hi[:, d, :].bitcast(fp32), op0=ALU.max,
                                         op1=ALU.subtract).then_inc(job_taken[j], 1)

            def take_v(b, j):
                n = int(j[1])
                wait(dve, job_done[j], b + 1)
                wait(dve, attn_done[1], b - 1)
                dve.tensor_tensor(v_sb[b % 2][:, 2 * n:2 * n + 2, :], ps_job[BANK[j]][:, :].rearrange("p (t n) -> p t n", n=D),
                                  bv_row[:, :].unsqueeze(1).to_broadcast([P, 2, D]), ALU.add).then_inc(job_taken[j], 1)

            def invert(b, g):
                wait(dve, probs_ready, b * UNITS + (g + 1) * GU)
                wait(dve, job_done[f"s{g}"], b)
                dve.reciprocal(row_inv[:, g * GU:(g + 1) * GU], row_sum[:, g * GU:(g + 1) * GU]).then_inc(inv_ready[g], 1)

            def normalize(b, g):
                wait(dve, attn_done[g], b + 1)
                wait(dve, job_taken[f"s{g}"], b + 1)
                wait(dve, job_done["o1"], b)
                dve.tensor_tensor(attnT[g][:, :], ps_attn[:, :], inv_spread[g][:, :], ALU.mult).then_inc(attn_ready[g], 1)

            def take_out(b, j):
                n = int(j[1])
                wait(dve, job_done[j], b + 1)
                wait(dve, res_ready, b + 1)
                wait(dve, stored, b * 16)
                dve.tensor_tensor(y[:, 2 * n:2 * n + 2, :], ps_job[BANK[j]][:, :].rearrange("p (t n) -> p t n", n=D),
                                  x_bias[:, 2 * n:2 * n + 2, :], ALU.add).then_inc(job_taken[j], 1)

            def moments(b, t):
                if t == 0:
                    wait(dve, x_loaded, (b + 1) * 16)
                    wait(dve, normed_ready, b * TT)
                dve.bn_stats(stats[:, t, :], x_in[:, t, :]).then_inc(stats_ready, 1)

            def aggregate(b, t):
                wait(dve, stats_ready, b * TT + t + 1)
                dve.bn_aggr(mean_var[:, t, :], stats[:, t, :]).then_inc(mean_var_ready, 1)

            SIDE = {0: (normalize, -1, 0), 4: (low_part, 0, "q1"), 6: (low_part, 0, "k1"), 8: (take_v, 0, "v0"),
                    9: (invert, -1, 1), 10: (take_v, 0, "v1"), 12: (low_h, 1, "h0"), 14: (low_h, 1, "h1"),
                    16: (normalize, -1, 1), 18: (low_part, 1, "q0"), 20: (low_part, 1, "k0"),
                    22: (take_out, -1, "o0"), 24: (take_out, -1, "o1"), 25: (invert, 0, 0)}
            MOMENTS = {26: 0, 27: 1, 28: 2, 30: 3}
            for b in range(-2, B + 1):
                for slot in range(UNITS):
                    if has(b):
                        masked(b, slot)
                    u = (slot - LAG) % UNITS
                    its = b if slot >= LAG else b - 1
                    if has(its) and TAKER[u] == 0:
                        take_turned(its, u)
                    if slot in SIDE:
                        step, off, what = SIDE[slot]
                        if has(b + off):
                            step(b + off, what)
                    if slot in MOMENTS and has(b + 2):
                        moments(b + 2, MOMENTS[slot])
                    if slot - 1 in MOMENTS and has(b + 2):
                        aggregate(b + 2, MOMENTS[slot - 1])

        @block.scalar
        def _(act):
            act.wait_ge(scaled_ready, 2)

            def exponential(b, u):
                wait(act, masked_ready, b * UNITS + u + 1)
                wait(act, turned, b * UNITS + u - SR + 1)
                if u % GU == 0:
                    wait(act, inv_ready[u // GU], b)
                act.activation(probs[:, u % SR, :], scores[:, u % SR, :], ACT.Exp, bias=neg_max[:, u:u + 1],
                               scale=-1.0, accum_out=row_sum[:, u:u + 1]).then_inc(probs_ready, 1)

            def take_turned(b, u):
                g, j, t = u // GU, u % GU // TT, u % TT
                wait(act, turned, b * UNITS + u + 1)
                if u % GU == 1:
                    wait(act, attn_done[g], b)
                act.activation(probsT[g][:, j, :, t * P:(t + 1) * P],
                               ps_turn[u % 2][:, :].rearrange("p (k q) -> p k q", q=P),
                               ACT.Copy).then_inc(turn_taken[1], 1)

            def high_part(b, j):
                w, g = j[0], int(j[1])
                wait(act, job_done[j], b + 1)
                wait(act, stacked[1 - g], (b + g) * 16 * G * G)
                act.activation(part_hi[w], ps_job[BANK[j]][:, :], ACT.Identity,
                               bias=b_col[w][:, g:g + 1]).then_inc(job_hi[j], 1)

            def high_h(b, j):
                d = int(j[1])
                wait(act, job_done[j], b + 1)
                wait(act, job_done["v1"], b)
                act.activation(hT_hi[:, d, :], ps_job[BANK[j]][:, :], ACT.Relu).then_inc(job_hi[j], 1)

            def take_spread(b, g):
                j = f"s{g}"
                wait(act, job_done[j], b + 1)
                wait(act, attn_ready[g], b)
                act.activation(inv_spread[g][:, :], ps_job[BANK[j]][:, :], ACT.Copy).then_inc(job_taken[j], 1)

            SIDE = {3: (high_part, 0, "q1"), 5: (high_part, 0, "k1"), 11: (high_h, 1, "h0"),
                    13: (high_h, 1, "h1"), 15: (take_spread, -1, 1), 17: (high_part, 1, "q0"),
                    19: (high_part, 1, "k0"), 29: (take_spread, 0, 0)}
            for b in range(-1, B + 1):
                for slot in range(UNITS):
                    if has(b):
                        exponential(b, slot)
                    u = (slot - LAG) % UNITS
                    its = b if slot >= LAG else b - 1
                    if has(its) and TAKER[u] == 1:
                        take_turned(its, u)
                    if slot in SIDE:
                        step, off, what = SIDE[slot]
                        if has(b + off):
                            step(b + off, what)


_INS = ['x', 'adj', 'L0_gnn_Wq', 'L0_gnn_bq', 'L0_gnn_Wk', 'L0_gnn_bk', 'L0_gnn_Wv', 'L0_gnn_bv', 'L0_gnn_Wo',
        'L0_gnn_bo']


def kernel(**inputs):
    import numpy as _np
    import concourse.bacc as _bacc
    from concourse import mybir as _mybir
    from concourse.bass_utils import run_bass_kernel_spmd as _run

    nc = _bacc.Bacc("TRN2", target_bir_lowering=False, num_devices=1)
    arrays, args = {}, []
    for name in _INS:
        a = _np.ascontiguousarray(inputs[name])
        arrays[f"in_{name}_dram"] = a
        args.append(nc.dram_tensor(f"in_{name}_dram", a.shape, _mybir.dt.from_np(a.dtype), kind="ExternalInput").ap())
    args.append(nc.dram_tensor("out_0_dram", arrays["in_x_dram"].shape, _mybir.dt.float32, kind="ExternalOutput").ap())
    gnn_attention(nc, *args)
    r = _run(nc, [arrays], core_ids=[0])
    return r.results[0]["out_0_dram"]
```

```python
import math
from contextlib import ExitStack

import concourse.bass as bass
from concourse import mybir

HEADS = 8
MASKED = 1e9
EPS = 1e-5


def gnn_attention(nc, x, adj, Wq, bq, Wk, bk, Wv, bv, Wo, bo, out):
    fp32 = mybir.dt.float32
    fp32r = mybir.dt.float32r
    ALU = mybir.AluOpType
    ACT = mybir.ActivationFunctionType

    B, N, D = x.shape
    P = 128
    HD = D // HEADS
    TT = N // P
    DT = D // P
    G = P // HD
    UNITS = HEADS * TT
    GU = G * TT
    SCALE = 1.0 / math.sqrt(HD)
    LAG = 3
    SB = 2
    TB = 3
    STEPS = 6
    SR = 4
    assert N == 512 and D == 256 and UNITS == 32 and GU == 16 and UNITS % SR == 0

    JOB_AT = {0: "cq1b", 1: "ck1a", 2: "ck1b", 5: "cv0a", 6: "cv0b", 7: "cv1a", 8: "cv1b",
              9: "nh0", 11: "nh1", 13: "ps1", 15: "nq0a", 16: "nq0b", 17: "nk0a", 18: "nk0b",
              21: "po0a", 22: "po0b", 23: "po1a", 24: "po1b", 28: "cs0", 31: "nq1a"}
    EARLY = 7
    V_TAKEN = 3
    WARM_UP = 40
    NEXT = {"p": -1, "c": 0, "n": 1}
    OFFSET = {j[1:3]: NEXT[j[0]] for j in JOB_AT.values() if j[3:] != "a"}
    JOBS = list(OFFSET)
    BANK = {j: i % 2 for i, j in enumerate(JOBS)}
    PV_AT = {4: (1, 0), 10: (1, 1), 12: (1, 2), 14: (1, 3), 20: (0, 0), 25: (0, 1), 26: (0, 2), 30: (0, 3)}
    TAKER = [1 if (u + LAG) % 2 == 0 or u + LAG in (5, 21, 27) else 0 for u in range(UNITS)]
    FIRST = [[TAKER.index(by, g * GU) for g in range(DT)] for by in range(2)]

    x_tiles = x.rearrange("b (t p) d -> b p t d", p=P)
    out_tiles = out.rearrange("b (t p) d -> b p t d", p=P)

    ctx = ExitStack()
    with ctx:
        def sb(name, shape, dt=fp32):
            return ctx.enter_context(nc.sbuf_tensor(name, shape, dt))

        def sem(name):
            return ctx.enter_context(nc.semaphore(name))

        ident = sb("ident", [P, P])
        mask = sb("mask", [P, TT, N])
        w_raw = {w: sb(f"w{w}_raw", [P, DT, D]) for w in "qkvo"}
        w_hi = {w: sb(f"w{w}_hi", [P, DT, D], fp32r) for w in "qkvo"}
        w_lo = {w: sb(f"w{w}_lo", [P, DT, D], fp32r) for w in "qkvo"}
        b_col = {w: sb(f"b{w}_col", [P, DT]) for w in "qk"}
        bv_row = sb("bv_row", [P, D])
        bo_row = sb("bo_row", [P, D])
        x_in = sb("x_in", [P, TT, D])
        stats = sb("stats", [P, TT, 6])
        mean_var = sb("mean_var", [P, TT, 2])
        var_eps = sb("var_eps", [P, TT])
        minus_half = sb("minus_half", [P, TT])
        rs_guess = sb("rs_guess", [P, TT])
        rs_square = sb("rs_square", [P, TT])
        rs_error = sb("rs_error", [P, TT])
        rs_factor = sb("rs_factor", [P, TT])
        rstd = sb("rstd", [P, TT])
        normed = sb("normed", [P, TT, D])
        hT_hi = sb("hT_hi", [P, DT, N], fp32r)
        hT_lo = sb("hT_lo", [P, DT, N], fp32r)
        parts = [sb(f"parts{g}", [P, 4, N], fp32r) for g in range(DT)]
        part_hi = {f"{w}{g}": parts[g][:, i, :] for g in range(DT) for w, i in (("q", 0), ("k", 3))}
        part_lo = {f"{w}{g}": parts[g][:, i, :] for g in range(DT) for w, i in (("q", 1), ("k", 2))}
        stacks = [sb(f"stacks{g}", [P, 2, G, N], fp32r) for g in range(DT)]
        v_sb = [sb(f"v_sb{i}", [P, TT, D]) for i in range(2)]
        scores = sb("scores", [P, SR, N])
        neg_max = sb("neg_max", [P, UNITS])
        probs = sb("probs", [P, SR, N])
        row_sum = sb("row_sum", [P, UNITS])
        row_inv = sb("row_inv", [P, UNITS])
        probsT = [sb(f"probsT{g}", [P, G, TT, N]) for g in range(DT)]
        inv_wide = sb("inv_wide", [P, TT, P])
        inv_spread = sb("inv_spread", [P, N])
        attnT = sb("attnT", [P, N])
        attnT_hi = [sb(f"attnT_hi{g}", [P, N], fp32r) for g in range(DT)]
        attnT_lo = [sb(f"attnT_lo{g}", [P, N], fp32r) for g in range(DT)]
        y = sb("y", [P, TT, D])

        def bank(name):
            return ctx.enter_context(nc.psum_tensor(name, [P, N], fp32))

        ps_scores = [bank(f"ps_scores{i}") for i in range(SB)]
        ps_turn = [bank(f"ps_turn{i}") for i in range(TB)]
        ps_attn = bank("ps_attn")
        ps_job = [bank(f"ps_job{i}") for i in range(2)]

        loaded = {n: sem(f"loaded_{n}") for n in ("Wq", "Wk", "Wv", "Wo", "bqk", "bv", "bo", "adj")}
        ident_ready = sem("ident_ready")
        consts_ready = sem("consts_ready")
        scaled_ready = sem("scaled_ready")
        split_hi_ready = sem("split_hi_ready")
        weights_ready = sem("weights_ready")
        x_loaded = sem("x_loaded")
        x_first = [sem(f"x_first{t}") for t in range(TT)]
        res_loaded = sem("res_loaded")
        stats_ready = sem("stats_ready")
        mean_var_ready = sem("mean_var_ready")
        rs_step = sem("rs_step")
        normed_ready = sem("normed_ready")
        res_ready = sem("res_ready")
        job_done = {j: sem(f"job_done_{j}") for j in JOBS}
        job_hi = {j: sem(f"job_hi_{j}") for j in JOBS if j[0] in "qkh"}
        job_taken = {j: sem(f"job_taken_{j}") for j in JOBS}
        stacked = [[sem(f"stacked{g}_{j}") for j in range(G)] for g in range(DT)]
        scores_done = sem("scores_done")
        masked_ready = sem("masked_ready")
        probs_ready = sem("probs_ready")
        turned = sem("turned")
        turn_taken = [sem("turn_taken_dve"), sem("turn_taken_act")]
        inv_ready = [sem(f"inv_ready{g}") for g in range(DT)]
        inv_widened = [sem(f"inv_widened{g}") for g in range(DT)]
        attn_done = [sem(f"attn_done{g}") for g in range(DT)]
        attn_hi_ready = [sem(f"attn_hi_ready{g}") for g in range(DT)]
        attn_split = [sem(f"attn_split{g}") for g in range(DT)]
        attn_ready = [sem(f"attn_ready{g}") for g in range(DT)]
        stored = sem("stored")

        def taken(b, u, by):
            return b * TAKER.count(by) + TAKER[:u].count(by)

        def job_before(b, j):
            at = (b - OFFSET[j]) * len(JOBS) + JOBS.index(j) - 2
            while at > -len(JOBS):
                before = JOBS[at % len(JOBS)]
                its = at // len(JOBS) + OFFSET[before]
                if has(its):
                    return before, its
                at -= 2
            return j, -1

        def wait(eng, s, value):
            if not isinstance(value, int) or value > 0:
                eng.wait_ge(s, value)

        def has(b):
            return 0 <= b < B

        def split_attention(eng, b, g):
            wait(eng, attn_ready[g], b + 1)
            wait(eng, job_done["o1"], b)
            eng.tensor_copy(attnT_hi[g][:, :], attnT[:, :]).then_inc(attn_hi_ready[g], 1)
            wait(eng, attn_hi_ready[g], b + 1)
            eng.tensor_tensor(attnT_lo[g][:, :], attnT[:, :], attnT_hi[g][:, :].bitcast(fp32),
                              ALU.subtract).then_inc(attn_split[g], 1)

        block = ctx.enter_context(nc.Block())

        @block.sync
        def _(sp):
            for t in range(TT):
                sp.dma_start(x_in[:, t, :], x_tiles[0][:, t, :]).then_inc(x_first[t], 16)

            def load_weight(w, src):
                sp.dma_start(w_raw[w][:, :, :], src.rearrange("(t p) n -> p t n", p=P)).then_inc(loaded["W" + w], 16)

            load_weight("k", Wk)
            load_weight("q", Wq)
            for w, src in (("q", bq), ("k", bk)):
                sp.dma_start(b_col[w][:, :], src.rearrange("(t p) -> p t", p=P),
                             allow_slow_non_contiguous=True).then_inc(loaded["bqk"], 16)
            sp.dma_start(mask[:, :, :], adj.rearrange("(t p) k -> p t k", p=P)).then_inc(loaded["adj"], 16)
            load_weight("v", Wv)
            sp.dma_start(bv_row[:, :], bv.partition_broadcast(P)).then_inc(loaded["bv"], 16)
            load_weight("o", Wo)
            sp.dma_start(bo_row[:, :], bo.partition_broadcast(P)).then_inc(loaded["bo"], 16)

            def stack_up(b, g):
                wait(sp, scores_done, (b - 1) * UNITS + (g + 1) * GU)
                wait(sp, job_taken[f"q{g}"], b + 1)
                wait(sp, job_taken[f"k{g}"], b + 1)
                for j in range(G):
                    for r, (a, z, step) in enumerate(((0, 4, 3), (0, 3, 2), (1, 4, 2), (1, 3, 1))):
                        row_tile, head = slice(r * HD, (r + 1) * HD), slice(j * HD, (j + 1) * HD)
                        sp.dma_start(stacks[g][row_tile, :, j, :].bitcast(fp32),
                                     parts[g][head, a:z:step, :].bitcast(fp32)).then_inc(stacked[g][j], 16)

            def load_x(b):
                wait(sp, normed_ready, b * TT)
                sp.dma_start(x_in[:, :, :], x_tiles[b]).then_inc(x_loaded, 16)

            def load_residual(b):
                wait(sp, stored, 32 * b)
                sp.dma_start(y[:, :, :], x_tiles[b]).then_inc(res_loaded, 16)

            def store(b):
                for n in range(2):
                    wait(sp, job_taken[f"o{n}"], b + 1)
                    tiles = slice(2 * n, 2 * n + 2)
                    sp.dma_start(out_tiles[b][:, tiles, :], y[:, tiles, :]).then_inc(stored, 16)

            for b in range(-1, B + 1):
                if has(b - 1):
                    load_residual(b - 1)
                if has(b):
                    stack_up(b, 1)
                if has(b + 2):
                    load_x(b + 2)
                if has(b + 1):
                    stack_up(b + 1, 0)
                if has(b - 1):
                    store(b - 1)
            sp.wait_ge(stored, 32 * B)

        @block.gpsimd
        def _(pool):
            pool.memset(ident[:, :], 0.0).then_inc(ident_ready, 1)
            pool.wait_ge(ident_ready, 1)
            pool.affine_select(out=ident[:, :], in_=ident[:, :], compare_op=ALU.not_equal, fill=1.0,
                               base=0, pattern=[[-1, P]], channel_multiplier=1).then_inc(ident_ready, 1)
            pool.memset(minus_half[:, :], -0.5).then_inc(consts_ready, 1)
            pool.wait_ge(consts_ready, 1)

            def inverse_deviation(b):
                done = b * STEPS
                wait(pool, mean_var_ready, (b + 1) * TT)
                pool.tensor_scalar(var_eps[:, :], mean_var[:, :, 1], EPS, None, ALU.add).then_inc(rs_step, 1)
                wait(pool, rs_step, done + 1)
                pool.tensor_tensor(rs_guess[:, :], var_eps[:, :], minus_half[:, :], ALU.pow).then_inc(rs_step, 1)
                wait(pool, rs_step, done + 2)
                pool.tensor_tensor(rs_square[:, :], rs_guess[:, :], rs_guess[:, :], ALU.mult).then_inc(rs_step, 1)
                wait(pool, rs_step, done + 3)
                pool.tensor_tensor(rs_error[:, :], rs_square[:, :], var_eps[:, :], ALU.mult).then_inc(rs_step, 1)
                wait(pool, rs_step, done + 4)
                pool.tensor_scalar(rs_factor[:, :], rs_error[:, :], -0.5, 1.5, ALU.mult, ALU.add).then_inc(rs_step, 1)
                wait(pool, rs_step, done + 5)
                pool.tensor_tensor(rstd[:, :], rs_guess[:, :], rs_factor[:, :], ALU.mult).then_inc(rs_step, 1)

            def norm(b):
                wait(pool, rs_step, (b + 1) * STEPS)
                wait(pool, job_done["h1"], b)
                for t in range(TT):
                    pool.tensor_scalar(normed[:, t, :], x_in[:, t, :], mean_var[:, t, 0:1], rstd[:, t:t + 1],
                                       ALU.subtract, ALU.mult).then_inc(normed_ready, 1)

            def residual(b):
                wait(pool, res_loaded, 16 * (b + 1))
                pool.wait_ge(loaded["bo"], 16)
                pool.tensor_tensor(y[:, :, :], y[:, :, :],
                                   bo_row[:, :].unsqueeze(1).to_broadcast([P, TT, D]), ALU.add).then_inc(res_ready, 1)

            def widen(b, g):
                wait(pool, inv_ready[g], b + 1)
                wait(pool, job_done[f"s{1 - g}"], b + g)
                inv = row_inv[:, g * GU:(g + 1) * GU].rearrange("p (i t) -> p t i", t=TT)
                pool.tensor_copy(inv_wide[:, :, :].rearrange("p t (i d) -> p t i d", d=HD),
                                 inv.unsqueeze(3).to_broadcast([P, TT, G, HD])).then_inc(inv_widened[g], 1)

            inverse_deviation(0)
            for b in range(-1, B + 1):
                if has(b - 1):
                    residual(b - 1)
                    widen(b - 1, 1)
                    if has(b):
                        split_attention(pool, b - 1, 0)
                        split_attention(pool, b - 1, 1)
                if has(b):
                    widen(b, 0)
                if has(b + 2):
                    inverse_deviation(b + 2)
                    norm(b + 2)

        @block.tensor
        def _(pe):
            pe.wait_ge(ident_ready, 2)
            for _ in range(WARM_UP):
                pe.transpose(ps_job[0][:, :P], ident[:, :], ident[:, :])

            def score(b, u):
                g, j, t = u // GU, u % GU // TT, u % TT
                if t == 0:
                    wait(pe, stacked[g][j], (b + 1) * 16 * G)
                wait(pe, masked_ready, b * UNITS + u + 1 - SB)
                pe.matmul(ps_scores[(b * UNITS + u) % SB][:, :], stacks[g][:, 0, j, t * P:(t + 1) * P],
                          stacks[g][:, 1, j, :], start=True, stop=True).then_inc(scores_done, 1)

            def turn(b, u):
                wait(pe, probs_ready, b * UNITS + u + 1)
                last = (u - TB) % UNITS
                by = TAKER[last]
                wait(pe, turn_taken[by], taken(b if u >= TB else b - 1, last + 1, by))
                for k in range(TT):
                    block_k = slice(k * P, (k + 1) * P)
                    mm = pe.transpose(ps_turn[(b * UNITS + u) % TB][:, block_k], probs[:, u % SR, block_k],
                                      ident[:, :])
                mm.then_inc(turned, 1)

            def attend(b, g, k):
                if k == 0:
                    for by in range(2):
                        wait(pe, turn_taken[by], taken(b, (g + 1) * GU, by))
                    wait(pe, job_taken["v0"], b + 1)
                    wait(pe, job_taken["v1"], b + 1)
                    wait(pe, attn_ready[1 - g], b + g)
                for j in range(G):
                    h = g * G + j
                    mm = pe.matmul(ps_attn[j * HD:(j + 1) * HD, :], v_sb[b % 2][:, k, h * HD:(h + 1) * HD],
                                   probsT[g][:, j, k, :], start=(k == 0), stop=(k == TT - 1))
                if k == TT - 1:
                    mm.then_inc(attn_done[g], 1)

            def split_products(dst, pairs, first=True, last=True):
                todo = [(a, r) for (ah, al), (rh, rl) in pairs for a, r in ((ah, rh), (ah, rl), (al, rh))]
                for n, (a, r) in enumerate(todo):
                    mm = pe.matmul(dst, a, r, start=(first and n == 0), stop=(last and n == len(todo) - 1))
                return mm

            def job(b, j, halves):
                kind, n = j[0], int(j[1])
                dst = ps_job[BANK[j]]
                if 0 in halves:
                    before, its = job_before(b, j)
                    wait(pe, job_taken[before], its + 1)
                if kind == "h":
                    for t in range(TT):
                        wait(pe, normed_ready, b * TT + t + 1)
                        mm = pe.transpose(dst[:, t * P:(t + 1) * P], normed[:, t, n * P:(n + 1) * P], ident[:, :])
                elif kind in "qk":
                    wait(pe, weights_ready, 2)
                    cols = slice(n * P, (n + 1) * P)
                    for d in halves:
                        wait(pe, job_taken[f"h{d}"], b + 1)
                        mm = split_products(dst[:, :], [((w_hi[kind][:, d, cols], w_lo[kind][:, d, cols]),
                                                         (hT_hi[:, d, :], hT_lo[:, d, :]))], d == 0, d == DT - 1)
                elif kind == "v":
                    wait(pe, weights_ready, 3)
                    for i in halves:
                        rows = slice((2 * n + i) * P, (2 * n + i + 1) * P)
                        mm = split_products(dst[:, i * D:(i + 1) * D],
                                            [((hT_hi[:, d, rows], hT_lo[:, d, rows]),
                                              (w_hi["v"][:, d, :], w_lo["v"][:, d, :])) for d in range(DT)])
                elif kind == "s":
                    wait(pe, inv_widened[n], b + 1)
                    for t in range(TT):
                        mm = pe.transpose(dst[:, t * P:(t + 1) * P], inv_wide[:, t, :], ident[:, :])
                elif kind == "o":
                    wait(pe, weights_ready, 4)
                    whole = b == B - 1
                    wait(pe, attn_split[0], b + 1)
                    wait(pe, attn_ready[1] if whole else attn_split[1], b + 1)
                    for i in halves:
                        rows = slice((2 * n + i) * P, (2 * n + i + 1) * P)
                        here = dst[:, i * D:(i + 1) * D]
                        mm = split_products(here, [((attnT_hi[g][:, rows], attnT_lo[g][:, rows]),
                                                    (w_hi["o"][:, g, :], w_lo["o"][:, g, :]))
                                                   for g in range(1 if whole else DT)], last=not whole)
                        if whole:
                            mm = pe.matmul(here, attnT[:, rows], w_raw["o"][:, 1, :], start=False, stop=True)
                if 1 in halves:
                    mm.then_inc(job_done[j], 1)

            def side_work(b, slot):
                if slot in PV_AT:
                    g, k = PV_AT[slot]
                    if has(b - g):
                        attend(b - g, g, k)
                if slot in JOB_AT:
                    j, half = JOB_AT[slot][1:3], JOB_AT[slot][3:]
                    its = b + NEXT[JOB_AT[slot][0]]
                    if has(its):
                        job(its, j, {"": (0, 1), "a": (0,), "b": (1,)}[half])

            for b in range(-1, B + 1):
                for slot in range(UNITS):
                    if has(b):
                        score(b, slot)
                    its = b if slot >= LAG else b - 1
                    if has(its):
                        turn(its, (slot - LAG) % UNITS)
                    if b != 0 or slot >= EARLY:
                        side_work(b, slot)
                if b == -1:
                    for slot in range(EARLY):
                        side_work(0, slot)

        @block.vector
        def _(dve):
            def masked(b, u):
                wait(dve, scores_done, b * UNITS + u + 1)
                wait(dve, probs_ready, b * UNITS + u - SR + 1)
                dve.tensor_tensor_reduce(scores[:, u % SR, :], ps_scores[(b * UNITS + u) % SB][:, :],
                                         mask[:, u % TT, :], 1.0, 3e38, ALU.add, ALU.min,
                                         neg_max[:, u:u + 1]).then_inc(masked_ready, 1)

            def take_turned(b, u):
                g, j, t = u // GU, u % GU // TT, u % TT
                wait(dve, turned, b * UNITS + u + 1)
                if u == FIRST[0][g]:
                    wait(dve, attn_done[g], b)
                dve.tensor_copy(probsT[g][:, j, :, t * P:(t + 1) * P],
                                ps_turn[(b * UNITS + u) % TB][:, :].rearrange("p (k q) -> p k q",
                                                                              q=P)).then_inc(turn_taken[0], 1)

            def low_part(b, j):
                w, g = j[0], int(j[1])
                wait(dve, job_hi[j], b + 1)
                dve.scalar_tensor_tensor(out=part_lo[j], in0=ps_job[BANK[j]][:, :], scalar=b_col[w][:, g:g + 1],
                                         in1=part_hi[j].bitcast(fp32), op0=ALU.add,
                                         op1=ALU.subtract).then_inc(job_taken[j], 1)

            def low_h(b, j):
                d = int(j[1])
                wait(dve, job_hi[j], b + 1)
                dve.scalar_tensor_tensor(out=hT_lo[:, d, :], in0=ps_job[BANK[j]][:, :], scalar=0.0,
                                         in1=hT_hi[:, d, :].bitcast(fp32), op0=ALU.max,
                                         op1=ALU.subtract).then_inc(job_taken[j], 1)

            def take_v(b, j):
                n = int(j[1])
                wait(dve, job_done[j], b + 1)
                wait(dve, attn_done[1], b - 1)
                dve.tensor_tensor(v_sb[b % 2][:, 2 * n:2 * n + 2, :],
                                  ps_job[BANK[j]][:, :].rearrange("p (t n) -> p t n", n=D),
                                  bv_row[:, :].unsqueeze(1).to_broadcast([P, 2, D]), ALU.add).then_inc(job_taken[j], 1)

            def invert(b, g):
                wait(dve, probs_ready, b * UNITS + (g + 1) * GU)
                wait(dve, inv_widened[g], b)
                dve.reciprocal(row_inv[:, g * GU:(g + 1) * GU],
                               row_sum[:, g * GU:(g + 1) * GU]).then_inc(inv_ready[g], 1)

            def normalize(b, g):
                wait(dve, attn_done[g], b + 1)
                wait(dve, job_taken[f"s{g}"], b + 1)
                wait(dve, attn_split[1 - g], b + g)
                dve.tensor_tensor(attnT[:, :], ps_attn[:, :], inv_spread[:, :], ALU.mult).then_inc(attn_ready[g], 1)

            def take_out(b, j):
                n = int(j[1])
                wait(dve, job_done[j], b + 1)
                wait(dve, res_ready, b + 1)
                dve.tensor_tensor(y[:, 2 * n:2 * n + 2, :], ps_job[BANK[j]][:, :].rearrange("p (t n) -> p t n", n=D),
                                  y[:, 2 * n:2 * n + 2, :], ALU.add).then_inc(job_taken[j], 1)

            def moments(b, t):
                if b == 0:
                    dve.wait_ge(x_first[t], 16)
                elif t == 0:
                    wait(dve, x_loaded, b * 16)
                    wait(dve, normed_ready, b * TT)
                dve.bn_stats(stats[:, t, :], x_in[:, t, :]).then_inc(stats_ready, 1)

            def aggregate(b, t):
                wait(dve, stats_ready, b * TT + t + 1)
                dve.bn_aggr(mean_var[:, t, :], stats[:, t, :]).then_inc(mean_var_ready, 1)

            SIDE = {0: (normalize, -1, 0), 2: (low_part, 0, "q1"), 4: (low_part, 0, "k1"), 8: (take_v, 0, "v0"),
                    9: (invert, -1, 1), 10: (take_v, 0, "v1"), 12: (low_h, 1, "h0"), 14: (low_h, 1, "h1"),
                    16: (normalize, -1, 1), 18: (low_part, 1, "q0"), 20: (low_part, 1, "k0"),
                    24: (take_out, -1, "o0"), 26: (take_out, -1, "o1"), 25: (invert, 0, 0)}
            MOMENTS = {22: 0, 27: 1, 28: 2, 29: 3}

            def side_work(b, slot):
                if slot in SIDE:
                    step, off, what = SIDE[slot]
                    if has(b + off):
                        step(b + off, what)

            def weight_low(w, n):
                dve.wait_ge(split_hi_ready, n)
                dve.tensor_tensor(w_lo[w][:, :, :], w_raw[w][:, :, :], w_hi[w][:, :, :].bitcast(fp32),
                                  ALU.subtract).then_inc(weights_ready, 1)

            for t in range(TT):
                moments(0, t)
                if t > 0:
                    aggregate(0, t - 1)
            aggregate(0, TT - 1)
            dve.wait_ge(loaded["Wq"], 16)
            dve.tensor_scalar(w_raw["q"][:, :, :], w_raw["q"][:, :, :], -SCALE, None,
                              ALU.mult).then_inc(scaled_ready, 1)
            weight_low("k", 1)
            dve.wait_ge(scaled_ready, 1)
            weight_low("q", 2)
            dve.wait_ge(loaded["bqk"], 32)
            dve.tensor_scalar(b_col["q"][:, :], b_col["q"][:, :], -SCALE, None, ALU.mult).then_inc(scaled_ready, 1)
            dve.wait_ge(rs_step, STEPS)
            for t in range(TT):
                dve.tensor_scalar(normed[:, t, :], x_in[:, t, :], mean_var[:, t, 0:1], rstd[:, t:t + 1],
                                  ALU.subtract, ALU.mult).then_inc(normed_ready, 1)
            dve.wait_ge(loaded["adj"], 16)
            dve.tensor_scalar(mask[:, :, :], mask[:, :, :], 1.0, -MASKED,
                              ALU.subtract, ALU.mult).then_inc(scaled_ready, 1)
            for b in range(-1, B + 1):
                for slot in range(UNITS):
                    if has(b):
                        masked(b, slot)
                    u = (slot - LAG) % UNITS
                    its = b if slot >= LAG else b - 1
                    if has(its) and TAKER[u] == 0:
                        take_turned(its, u)
                    if b != 0 or slot >= EARLY + V_TAKEN:
                        side_work(b, slot)
                    if b == -1 and slot == 14:
                        weight_low("v", 3)
                    if slot in MOMENTS and has(b + 2):
                        moments(b + 2, MOMENTS[slot])
                    if slot - 1 in MOMENTS and has(b + 2):
                        aggregate(b + 2, MOMENTS[slot - 1])
                    if b == B and slot == 9:
                        split_attention(dve, b - 1, 0)
                if b == -1:
                    dve.wait_ge(loaded["bv"], 16)
                    for slot in range(EARLY + V_TAKEN):
                        side_work(0, slot)
                    dve.wait_ge(scaled_ready, 3)
                if b == 0:
                    weight_low("o", 4)

        @block.scalar
        def _(act):
            def weight_high(w):
                act.wait_ge(loaded["W" + w], 16)
                act.activation(w_hi[w][:, :, :], w_raw[w][:, :, :], ACT.Copy).then_inc(split_hi_ready, 1)

            weight_high("k")
            act.wait_ge(scaled_ready, 1)
            weight_high("q")
            act.wait_ge(scaled_ready, 2)

            def exponential(b, u):
                wait(act, masked_ready, b * UNITS + u + 1)
                wait(act, turned, b * UNITS + u - SR + 1)
                if u % GU == 0:
                    wait(act, inv_ready[u // GU], b)
                act.activation(probs[:, u % SR, :], scores[:, u % SR, :], ACT.Exp, bias=neg_max[:, u:u + 1],
                               scale=-1.0, accum_out=row_sum[:, u:u + 1]).then_inc(probs_ready, 1)

            def take_turned(b, u):
                g, j, t = u // GU, u % GU // TT, u % TT
                wait(act, turned, b * UNITS + u + 1)
                if u == FIRST[1][g]:
                    wait(act, attn_done[g], b)
                act.activation(probsT[g][:, j, :, t * P:(t + 1) * P],
                               ps_turn[(b * UNITS + u) % TB][:, :].rearrange("p (k q) -> p k q", q=P),
                               ACT.Copy).then_inc(turn_taken[1], 1)

            def high_part(b, j):
                w, g = j[0], int(j[1])
                wait(act, job_done[j], b + 1)
                for head in range(G):
                    wait(act, stacked[g][head], b * 16 * G)
                act.activation(part_hi[j], ps_job[BANK[j]][:, :], ACT.Identity,
                               bias=b_col[w][:, g:g + 1]).then_inc(job_hi[j], 1)

            def high_h(b, j):
                d = int(j[1])
                wait(act, job_done[j], b + 1)
                wait(act, job_done["v1"], b)
                act.activation(hT_hi[:, d, :], ps_job[BANK[j]][:, :], ACT.Relu).then_inc(job_hi[j], 1)

            def take_spread(b, g):
                j = f"s{g}"
                wait(act, job_done[j], b + 1)
                wait(act, attn_ready[1 - g], b + g)
                act.activation(inv_spread[:, :], ps_job[BANK[j]][:, :], ACT.Copy).then_inc(job_taken[j], 1)

            SIDE = {1: (high_part, 0, "q1"), 3: (high_part, 0, "k1"), 11: (high_h, 1, "h0"),
                    13: (high_h, 1, "h1"), 15: (take_spread, -1, 1), 17: (high_part, 1, "q0"),
                    19: (high_part, 1, "k0"), 29: (take_spread, 0, 0)}

            def side_work(b, slot):
                if slot in SIDE:
                    step, off, what = SIDE[slot]
                    if has(b + off):
                        step(b + off, what)

            for b in range(-1, B + 1):
                for slot in range(UNITS):
                    if has(b):
                        exponential(b, slot)
                    u = (slot - LAG) % UNITS
                    its = b if slot >= LAG else b - 1
                    if has(its) and TAKER[u] == 1:
                        take_turned(its, u)
                    if b != 0 or slot >= EARLY:
                        side_work(b, slot)
                    if b == -1 and slot == 13:
                        weight_high("v")
                        weight_high("o")
                if b == -1:
                    for slot in range(EARLY):
                        side_work(0, slot)


_INS = ['x', 'adj', 'L0_gnn_Wq', 'L0_gnn_bq', 'L0_gnn_Wk', 'L0_gnn_bk', 'L0_gnn_Wv', 'L0_gnn_bv', 'L0_gnn_Wo',
        'L0_gnn_bo']


def kernel(**inputs):
    import numpy as _np
    import concourse.bacc as _bacc
    from concourse import mybir as _mybir
    from concourse.bass_utils import run_bass_kernel_spmd as _run

    nc = _bacc.Bacc("TRN2", target_bir_lowering=False, num_devices=1)
    arrays, args = {}, []
    for name in _INS:
        a = _np.ascontiguousarray(inputs[name])
        arrays[f"in_{name}_dram"] = a
        args.append(nc.dram_tensor(f"in_{name}_dram", a.shape, _mybir.dt.from_np(a.dtype), kind="ExternalInput").ap())
    args.append(nc.dram_tensor("out_0_dram", arrays["in_x_dram"].shape, _mybir.dt.float32, kind="ExternalOutput").ap())
    gnn_attention(nc, *args)
    r = _run(nc, [arrays], core_ids=[0])
    return r.results[0]["out_0_dram"]
```
